# Optimizing a Trainium2 kernel written in Bass

```python
import numpy as np
import jax
import jax.numpy as jnp

def _softmax(x, axis=-1):
    return jax.nn.softmax(x, axis=axis)

def _gelu(x):
    return jax.nn.gelu(x, approximate=True)

def _silu(x):
    return jax.nn.silu(x)

def _sigmoid(x):
    return jax.nn.sigmoid(x)

def _layernorm(x, axis=-1, eps=1e-05):
    m = jnp.mean(x, axis=axis, keepdims=True)
    v = jnp.var(x, axis=axis, keepdims=True)
    return (x - m) / jnp.sqrt(v + eps)

def _scatter_add(tgt, idx, src, axis=0):
    return tgt.at[idx].add(src)

def _segment_sum(src, seg, n):
    return jax.ops.segment_sum(src, seg, n)
kernel_name = 'mk_adj_preln_d4_adj_r2_058dcc'

def setup_inputs(seed: int=0):
    np.random.seed(seed)
    _w = jnp.asarray

    def _rec_inputs():
        import jax
        import jax.numpy as jnp
        _gk = jax.random.key(seed)
        x = -0.000929 + 1 * jax.random.normal(jax.random.fold_in(_gk, 1), (8192, 64), jnp.float32)
        _a = jax.random.bernoulli(jax.random.fold_in(_gk, 2), 0.00195312, (8192, 8192))
        _a = jnp.logical_or(_a, jnp.eye(8192, dtype=bool))
        _af = _a.astype(jnp.float32)
        _af = _af * jax.random.uniform(jax.random.fold_in(_gk, 3), (8192, 8192), jnp.float32, 0.05, 1)
        adj = _af
        return (x, adj)
    x, adj = _rec_inputs()

    def _L0_gnn_setup():
        import jax, jax.numpy as jnp
        import numpy as np
        HOP = 2
        N = 8192
        HIDDEN = 64
        key = jax.random.key(seed)
        k1, k2, k3 = jax.random.split(key, 3)
        user_embs = jax.random.normal(k1, (N, HIDDEN), dtype=jnp.float32)
        adj = jax.random.uniform(k2, (N, N), dtype=jnp.float32)
        limit = float(np.sqrt(6.0 / (2 * HIDDEN + HIDDEN)))
        W = jax.random.uniform(k3, (HOP, 2 * HIDDEN, HIDDEN), dtype=jnp.float32, minval=-limit, maxval=limit)
        return {'user_embs': user_embs, 'adj': adj, 'W': W}
    _L0_gnn_all = _L0_gnn_setup()
    _L0_gnn_in = {k: v for k, v in _L0_gnn_all.items() if k in ('W',)}
    del _L0_gnn_all

    def _L1_gnn_setup():
        import jax, jax.numpy as jnp
        import numpy as np
        N = 8192
        IN_F = 64
        OUT_F = 64
        key = jax.random.key(seed)
        k_x, k_adj, k_w = jax.random.split(key, 3)
        x = jax.random.normal(k_x, (N, IN_F), dtype=jnp.float32)
        adj = jax.random.uniform(k_adj, (N, N), dtype=jnp.float32)
        std = float(np.sqrt(2.0 / (IN_F + OUT_F)))
        weight = jax.random.normal(k_w, (IN_F, OUT_F), dtype=jnp.float32) * std
        bias = jnp.zeros((OUT_F,), dtype=jnp.float32)
        return {'x': x, 'adj': adj, 'weight': weight, 'bias': bias}
    _L1_gnn_all = _L1_gnn_setup()
    _L1_gnn_in = {k: v for k, v in _L1_gnn_all.items() if k in ('weight', 'bias')}
    del _L1_gnn_all

    def _L2_gnn_setup():
        import jax, jax.numpy as jnp
        import numpy as np
        P_DROP = 0.1
        key = jax.random.key(seed)
        k1, k2, k3 = jax.random.split(key, 3)
        N, D = (8192, 64)
        x = jax.random.normal(k1, (N, D), dtype=jnp.float32)
        adj = jax.random.uniform(k2, (N, N), dtype=jnp.float32)
        u = jax.random.uniform(k3, (N, D), dtype=jnp.float32)
        return {'x': x, 'adj': adj, 'u': u}
    _L2_gnn_all = _L2_gnn_setup()
    _L2_gnn_in = {k: v for k, v in _L2_gnn_all.items() if k in ('u',)}
    del _L2_gnn_all

    def _L3_gnn_setup():
        import jax, jax.numpy as jnp
        import numpy as np
        N = 8192
        F = 64
        O = 64
        key = jax.random.key(seed)
        k1, k2, k3 = jax.random.split(key, 3)
        features = jax.random.normal(k1, (N, F), dtype=jnp.float32)
        adj = jax.random.uniform(k2, (N, N), dtype=jnp.float32)
        W = jax.random.normal(k3, (O, 2 * F), dtype=jnp.float32)
        return {'features': features, 'adj': adj, 'W': W}
    _L3_gnn_all = _L3_gnn_setup()
    _L3_gnn_in = {k: v for k, v in _L3_gnn_all.items() if k in ('W',)}
    del _L3_gnn_all
    return {'x': x, 'adj': adj, 'L0_gnn_W': _L0_gnn_in['W'], 'L1_gnn_weight': _L1_gnn_in['weight'], 'L1_gnn_bias': _L1_gnn_in['bias'], 'L2_gnn_u': _L2_gnn_in['u'], 'L3_gnn_W': _L3_gnn_in['W']}

def reference(x, adj, L0_gnn_W, L1_gnn_weight, L1_gnn_bias, L2_gnn_u, L3_gnn_W):
    import jax
    import jax.numpy as jnp

    def _L0_gnn_ref(user_embs, adj, W):
        import jax, jax.numpy as jnp
        import numpy as np
        HOP = 2
        N = 8192
        HIDDEN = 64
        x = user_embs
        for k in range(HOP):
            agg = adj @ x
            x = jnp.tanh(jnp.concatenate([agg, x], axis=1) @ W[k])
        return x

    def _L1_gnn_ref(x, adj, weight, bias):
        import jax, jax.numpy as jnp
        import numpy as np
        N = 8192
        IN_F = 64
        OUT_F = 64
        support = jnp.matmul(x, weight)
        output = jnp.matmul(adj, support)
        return output + bias

    def _L2_gnn_ref(x, adj, u):
        import jax, jax.numpy as jnp
        import numpy as np
        P_DROP = 0.1
        keep = (u >= P_DROP).astype(x.dtype)
        x_drop = x * keep / (1.0 - P_DROP)
        return jnp.matmul(adj, x_drop)

    def _L3_gnn_ref(features, adj, W):
        import jax, jax.numpy as jnp
        import numpy as np
        N = 8192
        F = 64
        O = 64
        deg = jnp.sum(adj, axis=1, keepdims=True)
        neigh = adj @ features / (deg + 1.0)
        data = jnp.concatenate([features, neigh], axis=-1)
        return data @ W.T
    h = jnp.maximum(_layernorm(x, axis=-1), 0.0)
    x = x + _L0_gnn_ref(h, adj, L0_gnn_W)
    h = jnp.maximum(_layernorm(x, axis=-1), 0.0)
    x = x + _L1_gnn_ref(h, adj, L1_gnn_weight, L1_gnn_bias)
    h = jnp.maximum(_layernorm(x, axis=-1), 0.0)
    x = x + _L2_gnn_ref(h, adj, L2_gnn_u)
    h = jnp.maximum(_layernorm(x, axis=-1), 0.0)
    x = x + _L3_gnn_ref(h, adj, L3_gnn_W)
    return x

_drawn_inputs = setup_inputs


def setup_inputs(seed=0):
    import zlib

    import numpy as np

    out = dict(_drawn_inputs(seed))
    spreads = {'L1_gnn_bias': (0.0, 0.444)}
    factors = {}
    for name, (base, spread) in spreads.items():
        noise = np.random.default_rng([zlib.crc32(name.encode()), seed]).standard_normal(out[name].shape)
        drawn = base * np.exp(spread * noise) if base else spread * noise
        out[name] = jnp.asarray(drawn.astype(out[name].dtype))
    for name, factor in factors.items():
        out[name] = (out[name] * factor).astype(out[name].dtype)
    return out
```

```python
import concourse.bass as bass
from concourse import mybir
from contextlib import ExitStack

N = 8192
F = 64
P = 128
BLOCK = 512
NB = N // BLOCK
TPB = BLOCK // P
NT = N // P
SWEEPS = 5
GROUP = 16
NGROUPS = NT // GROUP
RING = 8
KEPT = 4
DEG_LEAD = 3
EPS = 1e-5
P_DROP = 0.1

WITH_OWN_OPERAND = (1, 2, 5)


class Row:

    def __init__(self, r):
        self.r = r
        self.sweep = r // NB + 1
        at = r % NB
        upwards = self.sweep % 2 == 0 or self.sweep == SWEEPS
        self.i = NB - 1 - at if upwards else at
        self.half = (self.sweep - 1) % 2
        i = self.i
        if self.sweep == 1:
            self.single, self.double = list(range(i, NB)), list(range(i))
        elif self.sweep == SWEEPS:
            self.single, self.double = list(range(i, -1, -1)), []
        elif self.sweep % 2 == 0:
            self.single, self.double = [i], list(range(NB - 1, i, -1))
        else:
            self.single, self.double = [i], list(range(i))
        self.own = self.sweep in WITH_OWN_OPERAND


ROWS = [Row(r) for r in range(SWEEPS * NB)]
ROW_OF = {(row.sweep, row.i): row for row in ROWS}


def partial_from_before(row):
    return row.sweep > 1 and bool(ROW_OF[row.sweep - 1, row.i].double)


def make_schedule():
    order, number = [], 0
    for row in ROWS:
        before = ROWS[row.r - 1] if row.r else None
        blocks = [(j, "single") for j in row.single] + [(j, "double") for j in row.double]
        post_at = {1: 5}.get(row.sweep, 1)
        if row.r % NB == 0 and row.sweep in (2, 3, 4):
            post_at = 0
        post_at = min(post_at, len(blocks))
        for n, (j, kind) in enumerate(blocks):
            if before and n == post_at:
                order.append(("post", before))
            order.append(("block", row, j, kind, number))
            number += 1
            if n == 0 and row.own:
                order.append(("turn", row))
            if row.sweep == 1 and row.r and n == 10:
                order.append(("degree", before))
        if before and post_at == len(blocks):
            order.append(("post", before))
        if row.r == NB:
            order.append(("degree", before))
    order.append(("post", ROWS[-1]))
    return order


SCHEDULE = make_schedule()
BLOCKS = [e for e in SCHEDULE if e[0] == "block"]


def place_blocks():
    places, in_ring, seen = [], 0, set()
    for _, row, j, _, _ in BLOCKS:
        if row.i == j and j < KEPT:
            places.append(("kept", j, j not in seen))
            seen.add(j)
        else:
            places.append(("ring", in_ring, True))
            in_ring += 1
    return places


PLACES = place_blocks()
RING_ORDER = [n for n, place in enumerate(PLACES) if place[0] == "ring"]


def is_last_single(row, j):
    return j == row.single[-1]


def used_with(row, kind):
    last = (row.single if kind == "single" else row.double)[-1]
    return 1 + next(number for _, of, j, _, number in BLOCKS if of is row and j == last)


def rows_with_doubles(r):
    return sum(bool(row.double) for row in ROWS[: r + 1])


def rows_with_own(r):
    return sum(row.own for row in ROWS[: r + 1])


def gnn_kernel(nc, adj, x, w_both, w_own, bias, u, identity, ones, out):
    f32 = mybir.dt.float32
    ALU = mybir.AluOpType
    ACT = mybir.ActivationFunctionType

    ctx = ExitStack()
    with ctx:
        def sb(name, shape):
            return ctx.enter_context(nc.sbuf_tensor(name, shape, f32))

        def bank(name):
            return ctx.enter_context(nc.psum_tensor(name, [P, BLOCK], f32))

        def sem(name):
            return ctx.enter_context(nc.semaphore(name))

        ring = sb("ring", [P, RING, TPB * BLOCK])
        kept = sb("kept", [P, KEPT, TPB * BLOCK])
        operand = sb("operand", [P, NT, 2 * F])
        partial = sb("partial", [P, NB, BLOCK])
        resid = sb("resid", [P, NT, F])
        w_both_sb = sb("w_both_sb", [P, SWEEPS, F])
        w_own_sb = sb("w_own_sb", [P, 2, F])
        bias_sb = sb("bias_sb", [P, F])
        ident = sb("ident", [P, P])
        ones_sb = sb("ones_sb", [P, 1])
        sums = sb("sums", [P, 2, BLOCK])
        own_t = sb("own_t", [P, 2, BLOCK])
        deg_part = sb("deg_part", [P, 2, 2 * BLOCK])
        deg_plus = sb("deg_plus", [P, TPB])
        rdeg = sb("rdeg", [P, NT])
        tanh_out = sb("tanh_out", [P, 2, TPB, F])
        u_in = sb("u_in", [P, 2, TPB, F])
        keep = sb("keep", [P, TPB, F])
        centred = sb("centred", [P, GROUP, F])
        stats = sb("stats", [P, GROUP, 6])
        moments = sb("moments", [P, GROUP, 2])
        sd = sb("sd", [P, GROUP])
        rsd = sb("rsd", [P, GROUP])
        eps = sb("eps", [P, 1])
        result = sb("result", [P, 2, TPB, F])

        double_acc = [bank(f"double_acc{i}") for i in range(2)]
        single_acc = [bank(f"single_acc{i}") for i in range(2)]
        natural = [bank(f"natural{i}") for i in range(2)]
        turn_acc = bank("turn_acc")
        deg_acc = bank("deg_acc")

        slot_loaded = [sem(f"slot_loaded{i}") for i in range(RING)]
        kept_loaded = [sem(f"kept_loaded{i}") for i in range(KEPT)]
        x_loaded = [sem(f"x_loaded{i}") for i in range(NGROUPS)]
        consts_loaded = sem("consts_loaded")
        u_loaded = [sem(f"u_loaded{i}") for i in range(2)]
        out_stored = [sem(f"out_stored{i}") for i in range(2)]
        eps_set = sem("eps_set")
        blocks_used = sem("blocks_used")
        turned = sem("turned")
        posted = sem("posted")
        deg_summed = sem("deg_summed")
        step = sem("step")
        deg_added = sem("deg_added")
        singles_taken = sem("singles_taken")
        sums_ready = sem("sums_ready")
        natural_taken = sem("natural_taken")
        deg_taken = sem("deg_taken")
        var_ready = sem("var_ready")
        first_ready = sem("first_ready")
        norm_ready = sem("norm_ready")
        others_taken = sem("others_taken")
        partial_saved = sem("partial_saved")
        own_ready = sem("own_ready")
        tanh_ready = sem("tanh_ready")
        sd_ready = sem("sd_ready")

        def stream_of(number):
            where, k, _ = PLACES[number]
            held = kept[:, k, :] if where == "kept" else ring[:, k % RING, :]
            return held.rearrange("p (t i) -> p t i", t=TPB)

        def wait_loaded(eng, number):
            where, k, _ = PLACES[number]
            if where == "kept":
                eng.wait_ge(kept_loaded[k], 16)
            else:
                eng.wait_ge(slot_loaded[k % RING], 16 * (k // RING + 1))

        def wait_operand(eng, sweep, j):
            if sweep == 1:
                eng.wait_ge(first_ready, j * TPB // GROUP + 1)
            elif sweep == 2:
                eng.wait_ge(tanh_ready, ROW_OF[1, j].r + 1)
            else:
                eng.wait_ge(norm_ready, ROW_OF[sweep - 1, j].r + 1 - NB)

        def tiles(i):
            return slice(i * TPB, (i + 1) * TPB)

        def half_of(half):
            return slice(half * F, (half + 1) * F)

        block = ctx.enter_context(nc.Block())

        @block.sync
        def _(sp):
            for number, (_, row, j, _, _) in enumerate(BLOCKS):
                where, k, fresh = PLACES[number]
                if where == "kept":
                    if fresh:
                        sp.dma_start(kept[:, k, :], adj[row.i, j]).then_inc(kept_loaded[k], 16)
                    continue
                if k >= RING:
                    last = RING_ORDER[k - RING]
                    sp.wait_ge(blocks_used, last + 1)
                    if last < NB * NB:
                        sp.wait_ge(deg_added, last + 1)
                sp.dma_start(ring[:, k % RING, :], adj[row.i, j]).then_inc(slot_loaded[k % RING], 16)

        @block.gpsimd
        def _(pool):
            for row in ROWS:
                if row.sweep == 4 - 1:
                    if row.r % NB >= 2:
                        pool.wait_ge(norm_ready, row.r - 2 + 1 - NB)
                    pool.dma_start(u_in[:, row.r % 2], u[:, tiles(row.i), :]).then_inc(u_loaded[row.r % 2], 16)
                if row.sweep == SWEEPS:
                    pool.wait_ge(natural_taken, row.r + 1 - 2 * NB)
                    pool.dma_start(out[:, tiles(row.i), :], result[:, row.r % 2]).then_inc(out_stored[row.r % 2], 16)
            for s in out_stored:
                pool.wait_ge(s, 16 * NB // 2)

        @block.tensor
        def _(pe):
            waited = {}

            def wait_new(semaphore, value):
                if waited.get(semaphore.name, 0) < value:
                    waited[semaphore.name] = value
                    pe.wait_ge(semaphore, value)

            class Waits:
                wait_ge = staticmethod(wait_new)

            def singles(row, j, number):
                acc = single_acc[row.r % 2]
                if j == row.single[0] and row.r >= 2:
                    wait_new(singles_taken, row.r - 1)
                    wait_new(others_taken, row.r - 1)
                stream = stream_of(number)
                for t in range(TPB):
                    column = t % 2
                    last = nc.tensor.matmul(
                        acc[half_of(column), :], operand[:, j * TPB + t, half_of(row.half)], stream[:, t, :],
                        start=j == row.single[0] and t < 2, stop=is_last_single(row, j) and t >= 2)
                return last

            def doubles(row, j, number):
                acc = double_acc[row.r % 2]
                if j == row.double[0] and row.r >= 2 and rows_with_doubles(row.r - 2):
                    wait_new(sums_ready, rows_with_doubles(row.r - 2))
                    wait_new(partial_saved, rows_with_doubles(row.r - 2))
                stream = stream_of(number)
                for t in range(TPB):
                    last = nc.tensor.matmul(
                        acc[:, :], operand[:, j * TPB + t, :], stream[:, t, :],
                        start=j == row.double[0] and t == 0, stop=j == row.double[-1] and t == TPB - 1)
                return last

            def turn(row):
                wait_operand(Waits, row.sweep, row.i)
                if rows_with_own(row.r) > 1:
                    wait_new(own_ready, rows_with_own(row.r) - 1)
                for t in range(TPB):
                    last = nc.tensor.matmul(
                        turn_acc[half_of(row.half), t * P:(t + 1) * P],
                        operand[:, row.i * TPB + t, half_of(row.half)], ident[:, :], start=True, stop=True)
                last.then_inc(turned, 1)

            def post(row):
                if row.double:
                    wait_new(sums_ready, rows_with_doubles(row.r))
                else:
                    wait_new(singles_taken, row.r + 1)
                wait_new(others_taken, row.r + 1)
                if row.own:
                    wait_new(own_ready, rows_with_own(row.r))
                if row.r >= 2:
                    before = ROWS[row.r - 2]
                    if before.sweep <= 2:
                        wait_new(tanh_ready, before.r + 1)
                    else:
                        wait_new(natural_taken, before.r + 1 - 2 * NB)
                acc = natural[row.r % 2]
                mixed = row.own and row.sweep != SWEEPS
                for t in range(TPB):
                    cut = slice(t * P, (t + 1) * P)
                    last = nc.tensor.matmul(
                        acc[:, t * F:(t + 1) * F], sums[:, row.r % 2, cut], w_both_sb[:, row.sweep - 1, :],
                        start=True, stop=not mixed)
                    if row.own:
                        to = (t + (0 if mixed else TPB)) * F
                        last = nc.tensor.matmul(
                            acc[:, to:to + F], own_t[half_of(row.half), row.r % 2, cut],
                            w_own_sb[half_of(row.half), row.sweep // SWEEPS, :], start=not mixed, stop=True)
                last.then_inc(posted, 1)

            def degree(row):
                wait_new(deg_added, (row.r + 1) * NB)
                if row.r:
                    wait_new(deg_taken, row.r)
                for t in range(TPB):
                    for s in range(2):
                        at = s * BLOCK + t * P
                        last = nc.tensor.matmul(
                            deg_acc[:, t:t + 1], deg_part[:, row.r % 2, at:at + P], ones_sb[:, :],
                            start=s == 0, stop=s == 1)
                last.then_inc(deg_summed, 1)

            wait_new(consts_loaded, 16 * 5)
            for what, row, *rest in SCHEDULE:
                if what == "block":
                    j, kind, number = rest
                    wait_operand(Waits, row.sweep, j)
                    if kind == "double":
                        wait_operand(Waits, row.sweep + 1, j)
                    wait_loaded(pe, number)
                    last = (singles if kind == "single" else doubles)(row, j, number)
                    last.then_inc(blocks_used, 1)
                elif what == "turn":
                    turn(row)
                elif what == "post":
                    post(row)
                else:
                    degree(row)

        @block.scalar
        def _(act):
            for g in range(NGROUPS):
                cut = slice(g * GROUP, (g + 1) * GROUP)
                act.dma_start(resid[:, cut, :], x[:, cut, :]).then_inc(x_loaded[g], 16)
            for to, of in ((w_both_sb, w_both), (w_own_sb, w_own), (bias_sb, bias), (ident, identity), (ones_sb, ones)):
                act.dma_start(to[:], of[:]).then_inc(consts_loaded, 16)

            deviations = [0]

            def deviation(n):
                deviations[0] += 1
                act.wait_ge(var_ready, deviations[0])
                nc.scalar.activation(sd[:, 0:n], moments[:, 0:n, 1], ACT.Sqrt, bias=eps[:, 0:1]).then_inc(sd_ready, 1)

            act.wait_ge(eps_set, 1)
            for g in range(NGROUPS):
                deviation(GROUP)
            for what, row, *rest in SCHEDULE:
                slot = row.r % 2
                if what == "block":
                    j, kind, _ = rest
                    if kind == "single" and is_last_single(row, j):
                        act.wait_ge(blocks_used, used_with(row, "single"))
                        other = half_of(1 - row.half)
                        nc.scalar.copy(sums[other, slot, :], single_acc[slot][other, :]).then_inc(others_taken, 1)
                    if kind == "double" and j == row.double[-1]:
                        act.wait_ge(blocks_used, used_with(row, "double"))
                        other = half_of(1 - row.half)
                        nc.scalar.copy(partial[other, row.i, :], double_acc[slot][other, :]).then_inc(partial_saved, 1)
                elif what == "turn":
                    act.wait_ge(turned, rows_with_own(row.r))
                    own = half_of(row.half)
                    nc.scalar.copy(own_t[own, slot, :], turn_acc[own, :]).then_inc(own_ready, 1)
                elif what == "post":
                    if row.sweep <= 2:
                        act.wait_ge(posted, row.r + 1)
                        got = natural[slot][:, 0:TPB * F].rearrange("p (t f) -> p t f", t=TPB)
                        to = operand[:, tiles(row.i), F:2 * F] if row.sweep == 1 else tanh_out[:, slot]
                        nc.scalar.activation(to, got, ACT.Tanh).then_inc(tanh_ready, 1)
                    if row.sweep in (2, 3, 4):
                        deviation(TPB)

        @block.vector
        def _(dve):
            steps = [0]

            def link(instruction):
                steps[0] += 1
                instruction.then_inc(step, 1)
                dve.wait_ge(step, steps[0])

            norms = [0]

            def normalize(values, n):
                for t in range(n):
                    last = nc.vector.bn_stats(stats[:, t, :], values[:, t, :])
                link(last)
                for t in range(n):
                    last = nc.vector.bn_aggr(moments[:, t, :], stats[:, t, :])
                last.then_inc(var_ready, 1)
                norms[0] += 1
                dve.wait_ge(sd_ready, norms[0])
                link(nc.vector.reciprocal(rsd[:, 0:n], sd[:, 0:n]))
                for t in range(n):
                    last = nc.vector.tensor_scalar(centred[:, t, :], values[:, t, :], moments[:, t, 0:1],
                                                   rsd[:, t:t + 1], ALU.subtract, ALU.mult)
                link(last)

            def first_operand(g):
                dve.wait_ge(x_loaded[g], 16)
                cut = slice(g * GROUP, (g + 1) * GROUP)
                normalize(resid[:, cut, :], GROUP)
                nc.vector.tensor_scalar_max(operand[:, cut, 0:F], centred[:, :, :], 0.0).then_inc(first_ready, 1)

            def add_degrees(number, row, j):
                acc = deg_part[:, row.r % 2, :]
                where, k, _ = PLACES[number]
                data = kept[:, k, :] if where == "kept" else ring[:, k % RING, :]
                if number % NB == 0 and row.r >= 2:
                    dve.wait_ge(deg_summed, row.r - 1)
                wait_loaded(dve, number)
                if number % NB == 0:
                    nc.vector.tensor_tensor(acc, data[:, 0:2 * BLOCK], data[:, 2 * BLOCK:], ALU.add)\
                        .then_inc(deg_added, 1)
                else:
                    link(nc.vector.tensor_tensor(acc, acc, data[:, 0:2 * BLOCK], ALU.add))
                    nc.vector.tensor_tensor(acc, acc, data[:, 2 * BLOCK:], ALU.add).then_inc(deg_added, 1)
                dve.wait_ge(deg_added, number + 1)

            def take_singles(row):
                dve.wait_ge(blocks_used, used_with(row, "single"))
                own = half_of(row.half)
                to, got = sums[own, row.r % 2, :], single_acc[row.r % 2][own, :]
                if partial_from_before(row):
                    dve.wait_ge(partial_saved, rows_with_doubles(ROW_OF[row.sweep - 1, row.i].r))
                    nc.vector.tensor_tensor(to, got, partial[own, row.i, :], ALU.add).then_inc(singles_taken, 1)
                else:
                    nc.vector.tensor_copy(to, got).then_inc(singles_taken, 1)

            def take_doubles(row):
                dve.wait_ge(blocks_used, used_with(row, "double"))
                dve.wait_ge(singles_taken, row.r + 1)
                own = half_of(row.half)
                to = sums[own, row.r % 2, :]
                nc.vector.tensor_tensor(to, double_acc[row.r % 2][own, :], to, ALU.add).then_inc(sums_ready, 1)

            def take_degrees(row):
                dve.wait_ge(deg_summed, row.r + 1)
                link(nc.vector.tensor_scalar_add(deg_plus[:, :], deg_acc[:, 0:TPB], 1.0))
                nc.vector.reciprocal(rdeg[:, tiles(row.i)], deg_plus[:, :]).then_inc(deg_taken, 1)

            def finish(row):
                slot, k = row.r % 2, row.r % NB
                got = natural[slot][:, 0:TPB * F].rearrange("p (t f) -> p t f", t=TPB)
                value = resid[:, tiles(row.i), :]
                if row.sweep == 2:
                    dve.wait_ge(tanh_ready, row.r + 1)
                    link(nc.vector.tensor_tensor(value, value, tanh_out[:, slot], ALU.add))
                if row.sweep == 3:
                    dve.wait_ge(u_loaded[slot], 16 * (k // 2 + 1))
                    dve.wait_ge(consts_loaded, 16 * 5)
                    nc.vector.tensor_scalar(keep[:, :, :], u_in[:, slot], P_DROP, 1.0 / (1.0 - P_DROP),
                                            ALU.is_ge, ALU.mult)
                    with_bias = bias_sb[:, :].unsqueeze(1).to_broadcast([P, TPB, F])
                    link(nc.vector.tensor_tensor(value, value, with_bias, ALU.add))
                if row.sweep in (3, 4):
                    dve.wait_ge(posted, row.r + 1)
                    nc.vector.tensor_tensor(value, got, value, ALU.add).then_inc(natural_taken, 1)
                    dve.wait_ge(natural_taken, row.r + 1 - 2 * NB)
                if row.sweep in (2, 4):
                    normalize(value, TPB)
                    nc.vector.tensor_scalar_max(operand[:, tiles(row.i), 0:F], centred[:, 0:TPB, :], 0.0)\
                        .then_inc(norm_ready, 1)
                if row.sweep == 3:
                    normalize(value, TPB)
                    nc.vector.scalar_tensor_tensor(operand[:, tiles(row.i), F:2 * F], centred[:, 0:TPB, :], 0.0,
                                                   keep[:, :, :], ALU.max, ALU.mult).then_inc(norm_ready, 1)
                if row.sweep == SWEEPS:
                    dve.wait_ge(posted, row.r + 1)
                    own = natural[slot][:, TPB * F:2 * TPB * F].rearrange("p (t f) -> p t f", t=TPB)
                    link(nc.vector.tensor_tensor(value, own, value, ALU.add))
                    if k >= 2:
                        dve.wait_ge(out_stored[slot], 16 * (k // 2))
                    for t in range(TPB):
                        at = row.i * TPB + t
                        last = nc.vector.scalar_tensor_tensor(result[:, slot, t], got[:, t, :], rdeg[:, at:at + 1],
                                                              value[:, t, :], ALU.mult, ALU.add)
                    last.then_inc(natural_taken, 1)

            nc.vector.memset(eps[:, :], EPS).then_inc(eps_set, 1)
            ahead = iter(e for e in BLOCKS if e[1].sweep == 1)

            def add_next_degrees():
                for _, row, j, _, number in ahead:
                    if number < NB and number * TPB % GROUP == 0:
                        first_operand(number * TPB // GROUP)
                    add_degrees(number, row, j)
                    return

            for _ in range(DEG_LEAD):
                add_next_degrees()
            for what, row, *rest in SCHEDULE:
                if what == "block":
                    add_next_degrees()
                    j, kind, _ = rest
                    if kind == "single" and is_last_single(row, j):
                        take_singles(row)
                    if kind == "double" and j == row.double[-1]:
                        take_doubles(row)
                elif what == "post":
                    if row.sweep > 1:
                        finish(row)
                elif what == "degree":
                    take_degrees(row)


def kernel(x, adj, L0_gnn_W, L1_gnn_weight, L1_gnn_bias, L2_gnn_u, L3_gnn_W):
    import numpy as np
    from concourse import bacc
    from concourse.bass_utils import run_bass_kernel_spmd

    def by_partition(a):
        return np.ascontiguousarray(np.asarray(a).reshape(NT, P, F).transpose(1, 0, 2))

    w0, w1 = np.asarray(L0_gnn_W)
    w3 = np.asarray(L3_gnn_W).T
    eye = np.eye(F, dtype=np.float32)
    both = [w0[:F], w1[:F], np.asarray(L1_gnn_weight), eye, w3[F:]]
    arrays = {
        "adj": np.ascontiguousarray(
            np.asarray(adj).reshape(NB, BLOCK, NB, TPB, P).transpose(0, 2, 4, 3, 1)
        ).reshape(NB, NB, P, TPB * BLOCK),
        "x": by_partition(x),
        "w_both": np.ascontiguousarray(np.stack([np.concatenate([w, w]) for w in both], axis=1)),
        "w_own": np.ascontiguousarray(np.stack([np.concatenate([w0[F:], w1[F:]]), np.concatenate([w3[:F], w3[:F]])], axis=1)),
        "bias": np.ascontiguousarray(np.broadcast_to(np.asarray(L1_gnn_bias), (P, F))),
        "u": by_partition(L2_gnn_u),
        "identity": np.eye(P, dtype=np.float32),
        "ones": np.ones((P, 1), np.float32),
    }
    nc = bacc.Bacc("TRN2", target_bir_lowering=False, num_devices=1)
    aps = {name: nc.dram_tensor("in_" + name, a.shape, mybir.dt.float32, kind="ExternalInput").ap()
           for name, a in arrays.items()}
    aps["out"] = nc.dram_tensor("out_rows", (P, NT, F), mybir.dt.float32, kind="ExternalOutput").ap()
    gnn_kernel(nc, **aps)
    got = run_bass_kernel_spmd(nc, [{"in_" + name: a for name, a in arrays.items()}], core_ids=[0])
    rows = got.results[0]["out_rows"]
    return np.ascontiguousarray(np.asarray(rows).transpose(1, 0, 2)).reshape(N, F)
```

```python
import concourse.bass as bass
from concourse import mybir
from contextlib import ExitStack

N = 8192
F = 64
P = 128
BLOCK = 512
NB = N // BLOCK
TPB = BLOCK // P
NT = N // P
SWEEPS = 5
GROUP = 4
NGROUPS = NT // GROUP
RING = 8
HELD = 3
KEPT = (14, 15)
FILL_UP = {2: (8, 9, 10, 11, 12, 13), 4: (10, 11, 12, 13)}
FILLS = {2: (1, 1, 3), 4: (1, 0, 2)}
FILL_DOWN = (3, 4, 5, 6)
RETAINED = tuple((NB - 1, j) for j in range(HELD))
FILL_LAST = tuple((NB - 1, j) for j in (3, 4, NB - 1))
DEGREES_LATER = (0,)
SHARE = 1.7
AHEAD = 6.0
EPS = 1e-5
P_DROP = 0.1

WITH_OWN_OPERAND = (1, 2, 5)


class Row:

    def __init__(self, r):
        self.r = r
        self.sweep = r // NB + 1
        at = r % NB
        upwards = self.sweep in (2, 4, 5)
        self.i = i = NB - 1 - at if upwards else at
        self.half = (self.sweep - 1) % 2
        self.own = self.sweep in WITH_OWN_OPERAND
        self.single = {1: [*range(i + 1, NB), i], 3: [] if i in FILL_DOWN else [i], 5: [*range(i, -1, -1)]}.get(self.sweep, [])
        self.double = {1: [*range(max(0, (i - 2) // 2 * 2), i)], 2: [*range(NB - 1, i, -1)], 3: [*range(i)], 4: [*range(NB - 1, i, -1)]}\
            .get(self.sweep, [])


ROWS = [Row(r) for r in range(SWEEPS * NB)]
ROW_OF = {(row.sweep, row.i): row for row in ROWS}


class Block:

    def __init__(self, number, row, j, kind, first, last):
        self.number, self.row, self.j, self.kind, self.first, self.last = number, row, j, kind, first, last


def make_plan():
    plan, count = [], [0]

    def blocks(row, js, kind, at=None):
        for n, j in enumerate(js):
            plan.extend((at or {}).get(n, []))
            plan.append(("block", Block(count[0], row, j, kind, n == 0, n == len(js) - 1)))
            count[0] += 1
        plan.extend((at or {}).get(len(js), []))

    def late(sweep, i, js):
        blocks(ROW_OF[sweep, i], js, "late")
        plan.append(("added", ROW_OF[sweep, i]))

    def early(i, js):
        blocks(ROW_OF[1, i], js, "early")
        plan.append(("added", ROW_OF[1, i]))

    def row_of(row, post_at, hoisted=False):
        n_single = 0 if hoisted else len(row.single)
        total = n_single + len(row.double)
        before = [("post", ROWS[row.r - 1])] if row.r % NB or row.sweep == SWEEPS else []
        if row.double:
            post_at = min(post_at, total - 1)
        at = {n: [] for n in range(total + 1)}
        if n_single == 0:
            at[0].append(("first", row))
        if row.own:
            at[min(1, n_single)].append(("turn", row))
        at[min(post_at, total)] += before
        if row.sweep == 3 and row.i >= 2 or row.r and ROWS[row.r - 1].sweep == 4 and ROWS[row.r - 1].i in DEGREES_LATER:
            at[min(2, total)].append(("degree", ROWS[row.r - 1]))
        if n_single:
            at[n_single].insert(0, ("first", row))
        if row.double:
            at[total].append(("doubles", row))
            if n_single:
                blocks(row, row.single, "single", {n: at[n] for n in range(n_single)})
            blocks(row, row.double, "double", {n - n_single: at[n] for n in range(n_single, total + 1)})
        else:
            blocks(row, row.single, "single", at)

    def upwards(sweep, beyond):
        bottom, before = ROW_OF[sweep, NB - 1], ROW_OF[sweep - 1, NB - 1]
        fill = [*FILL_UP[sweep]]
        fills = FILLS[sweep]

        def fill_with(n):
            for _ in range(n):
                i = fill.pop()
                late(sweep, i, [i])

        plan.append(("post", before))
        late(sweep, NB - 2, [NB - 2])
        fill_with(fills[0])
        late(sweep, NB - 1, [NB - 1])
        if bottom.own:
            plan.append(("turn", bottom))
        plan.append(("first", bottom))
        plan.append(("degree", before))
        fill_with(fills[1])
        plan.append(("post", bottom))
        fill_with(fills[2])
        for i in range(NB - 2, -1, -1):
            row = ROW_OF[sweep, i]
            if i >= NB - 3:
                plan.append(("first", row))
                if row.own:
                    plan.append(("turn", row))
                if i == NB - 3:
                    fill_with(len(fill))
                    plan.append(("post", ROWS[row.r - 1]))
                blocks(row, row.double, "double")
                plan.append(("doubles", row))
            else:
                row_of(row, 1)
            beyond(i)

    def downwards(row):
        if row.i >= 1 and row.i - 1 not in FILL_UP[row.sweep + 1] and row.i - 1 not in KEPT:
            late(row.sweep + 1, row.i - 1, [row.i - 1])

    for row in ROWS[:NB]:
        m = (row.i - 2) // 2
        below = [*range(2 * m + 4, NB)] if m >= 0 else []
        half = len(below) // 2
        mine = below[:half] if row.i % 2 == 0 else below[half:]
        start = 4 if row.i % 2 == 0 else 1
        gap = max(1.0, (len(row.single) - start) / max(1, len(mine)))
        given = 0
        for n, j in enumerate(row.single):
            plan.append(("block", Block(count[0], row, j, "single", n == 0, n == len(row.single) - 1)))
            count[0] += 1
            if n == 0:
                plan.append(("turn", row))
            if row.r and n == min(1, len(row.single) - 1):
                plan.append(("post", ROWS[row.r - 1]))
            if row.r and n == min(3, len(row.single) - 1):
                plan.append(("degree", ROWS[row.r - 1]))
            while given < len(mine) and (n + 1 >= start + given * gap or j == row.i):
                early(mine[given], [2 * m, 2 * m + 1])
                given += 1
        plan.append(("first", row))
        if row.double:
            blocks(row, row.double, "double")
            plan.append(("doubles", row))
        downwards(row)
    upwards(2, lambda i: None)

    first, second, third = ROWS[2 * NB: 2 * NB + 3]
    fill = [*FILL_DOWN]
    blocks(second, second.single, "single")
    plan.append(("post", ROWS[2 * NB - 1]))
    for i in fill[:2]:
        late(3, i, [i])
    blocks(first, first.single, "single")
    plan.append(("first", first))
    late(3, fill[2], [fill[2]])
    plan.append(("post", first))
    plan.append(("first", second))
    blocks(third, third.single, "single")
    late(3, fill[3], [fill[3]])
    blocks(second, second.double, "double")
    plan.append(("doubles", second))
    downwards(second)
    row_of(third, 0, hoisted=True)
    downwards(third)
    for row in ROWS[2 * NB + 3: 3 * NB]:
        row_of(row, 1)
        downwards(row)

    open_blocks = {i: [*range(i, -1, -1)] for i in range(NB)}
    due = [AHEAD]

    def some_of_sweep_5(i):
        due[0] += (NB - 1 - i) / SHARE
        ready = {k: [j for j in js if j >= i + 1 and (k, j) not in FILL_LAST] for k, js in open_blocks.items()}
        while due[0] >= 1 and any(ready.values()):
            k = max(ready, key=lambda k: (len(ready[k]), k))
            js = ready.pop(k)[: int(due[0])]
            due[0] -= len(js)
            open_blocks[k] = [j for j in open_blocks[k] if j not in js]
            late(SWEEPS, k, js)

    upwards(4, some_of_sweep_5)

    for row in ROWS[4 * NB:]:
        row.single = open_blocks[row.i]
        row_of(row, 1)
    plan.append(("post", ROWS[-1]))
    return plan


PLAN = make_plan()
BLOCKS = [block for what, block in PLAN if what == "block"]
ADDED = [row for what, row in PLAN if what == "added"]
DEGREE_BLOCKS = [
    b for b in BLOCKS
    if b.row.sweep == 1 and b.kind == "single" and (b.row.i not in DEGREES_LATER or b.j == b.row.i)
    or b.row.sweep == 4 and b.kind == "double" and b.row.i in DEGREES_LATER
    or b.row.sweep == 3 and b.kind == "double"]
DEGREE_ROWS = [row for what, row in PLAN if what == "degree"]


class Load:

    def __init__(self, place, slot, turn, first):
        self.place, self.slot, self.turn, self.uses = place, slot, turn, [first]


def make_loads():
    loads, of, kept, held, retained, turns = [], [], {}, {}, {}, {}
    for b in BLOCKS:
        i, j = b.row.i, b.j
        if i == j and i in KEPT and i in kept:
            load = kept[i]
            load.uses.append(b)
        elif i == j and b.kind == "late" and b.row.sweep < SWEEPS and i in held:
            load = held.pop(i)
            load.uses.append(b)
        elif (i, j) in retained:
            load = retained[i, j]
            load.uses.append(b)
        else:
            place = "ring"
            if i == j and i in KEPT:
                place = "kept"
            elif i == j and b.kind == "single" and b.row.sweep in (1, 3) and i not in FILL_UP[b.row.sweep + 1]:
                place = "held"
            elif b.row.sweep == 3 and (i, j) in RETAINED:
                place = "held"
            n = turns[place] = turns.get(place, -1) + 1
            size = {"ring": RING, "held": HELD, "kept": len(KEPT)}[place]
            load = Load(place, n % size, n // size, b)
            loads.append(load)
            if place == "kept":
                kept[i] = load
            elif place == "held" and i == j:
                held[i] = load
            elif place == "held":
                retained[i, j] = load
        of.append(load)
    return loads, of


LOADS, LOAD_OF = make_loads()


def used(row, kind):
    return next(b.number for b in BLOCKS if b.row is row and b.kind == kind and b.last) + 1


def rows_with_doubles(r):
    return sum(bool(row.double) for row in ROWS[: r + 1])


def rows_with_own(r):
    return sum(row.own for row in ROWS[: r + 1])


def added_to(row):
    return max([n + 1 for n, of in enumerate(ADDED) if of is row], default=0)


def kinds_with_banks():
    found, counts = [], {}
    for what, of in PLAN:
        if what in ("added", "turn", "degree"):
            found.append((what, counts.get(what, 0)))
            counts[what] = counts.get(what, 0) + 1
    return found


SPARE_USES = kinds_with_banks()


def gnn_kernel(nc, adj, x, w_both, w_own, bias, u, identity, ones, out):
    f32 = mybir.dt.float32
    ALU = mybir.AluOpType
    ACT = mybir.ActivationFunctionType

    ctx = ExitStack()
    with ctx:
        def sb(name, shape):
            return ctx.enter_context(nc.sbuf_tensor(name, shape, f32))

        def bank(name):
            return ctx.enter_context(nc.psum_tensor(name, [P, BLOCK], f32))

        def sem(name):
            return ctx.enter_context(nc.semaphore(name))

        ring = sb("ring", [P, RING, TPB * BLOCK])
        held = sb("held", [P, HELD, TPB * BLOCK])
        kept = sb("kept", [P, len(KEPT), TPB * BLOCK])
        operand = sb("operand", [P, NT, 2 * F])
        partial = sb("partial", [P, NB, BLOCK])
        resid = sb("resid", [P, NT, F])
        w_both_sb = sb("w_both_sb", [P, SWEEPS, F])
        w_own_sb = sb("w_own_sb", [P, 2, F])
        bias_sb = sb("bias_sb", [P, F])
        ident = sb("ident", [P, P])
        ones_sb = sb("ones_sb", [P, 1])
        sums = sb("sums", [P, 2, BLOCK])
        own_t = sb("own_t", [P, 2, BLOCK])
        deg_part = sb("deg_part", [P, 2, 2 * BLOCK])
        deg_plus = sb("deg_plus", [P, NT])
        rdeg = sb("rdeg", [P, NT])
        keep = sb("keep", [P, TPB, F])
        for_layer = sb("for_layer", [P, 2, TPB, F])
        tanh_out = for_layer
        u_in = for_layer
        result = for_layer
        centred = sb("centred", [P, GROUP, F])
        stats = sb("stats", [P, 2, GROUP, 6])
        moments = sb("moments", [P, 2, GROUP, 2])
        sd = sb("sd", [P, 2, GROUP])
        rsd = sb("rsd", [P, GROUP])
        eps = sb("eps", [P, 1])

        double_acc = [bank(f"double_acc{i}") for i in range(2)]
        single_acc = [bank(f"single_acc{i}") for i in range(2)]
        natural = [bank(f"natural{i}") for i in range(2)]
        spare = [bank(f"spare{i}") for i in range(2)]

        places = {"ring": ring, "held": held, "kept": kept}
        loaded = {"ring": [sem(f"ring_loaded{i}") for i in range(RING)],
                  "held": [sem(f"held_loaded{i}") for i in range(HELD)],
                  "kept": [sem(f"kept_loaded{i}") for i in range(len(KEPT))]}
        x_loaded = [sem(f"x_loaded{i}") for i in range(NGROUPS)]
        consts_loaded = sem("consts_loaded")
        u_loaded = [sem(f"u_loaded{i}") for i in range(2)]
        out_stored = [sem(f"out_stored{i}") for i in range(2)]
        eps_set = sem("eps_set")
        blocks_used = sem("blocks_used")
        turned = sem("turned")
        posted = sem("posted")
        deg_summed = sem("deg_summed")
        step = sem("step")
        deg_added = sem("deg_added")
        deg_folded = sem("deg_folded")
        first_taken = sem("first_taken")
        partial_added = sem("partial_added")
        added_taken = sem("added_taken")
        sums_ready = sem("sums_ready")
        natural_taken = sem("natural_taken")
        deg_taken = sem("deg_taken")
        var_ready = sem("var_ready")
        first_ready = sem("first_ready")
        norm_ready = sem("norm_ready")
        partial_saved = sem("partial_saved")
        own_ready = sem("own_ready")
        tanh_ready = sem("tanh_ready")
        sd_ready = sem("sd_ready")
        cleared = sem("cleared")

        def data_of(b):
            load = LOAD_OF[b.number]
            return places[load.place][:, load.slot, :]

        def wait_loaded(wait_ge, b):
            load = LOAD_OF[b.number]
            wait_ge(loaded[load.place][load.slot], 16 * (load.turn + 1))

        def wait_saved(wait_ge, r):
            first = rows_with_doubles(min(r, NB - 1))
            if r < NB and first:
                wait_ge(partial_added, first)
            if r >= NB and rows_with_doubles(r) > first:
                wait_ge(partial_saved, rows_with_doubles(r) - first)

        def wait_partial(wait_ge, row):
            if row.sweep == 1:
                wait_ge(cleared, 1)
                return
            before = ROW_OF[row.sweep - 1, row.i]
            if before.double:
                wait_saved(wait_ge, before.r)
            wait_ge(cleared, before.r + 3)

        def wait_operand(wait_ge, sweep, j):
            if sweep == 1:
                wait_ge(first_ready, j * TPB // GROUP + 1)
            elif sweep == 2:
                wait_ge(tanh_ready, ROW_OF[1, j].r + 1)
            else:
                wait_ge(norm_ready, ROW_OF[sweep - 1, j].r + 1 - NB)

        def tiles(i):
            return slice(i * TPB, (i + 1) * TPB)

        def half_of(half):
            return slice(half * F, (half + 1) * F)

        block = ctx.enter_context(nc.Block())

        @block.sync
        def _(sp):
            last_in = {}
            for n, load in enumerate(LOADS):
                b = load.uses[0]
                if n < NGROUPS:
                    for g in ([0, 1] if n == 0 else [n + 1] if n + 1 < NGROUPS else []):
                        cut = slice(g * GROUP, (g + 1) * GROUP)
                        sp.dma_start(resid[:, cut, :], x[:, cut, :]).then_inc(x_loaded[g], 16)
                old = last_in.get((load.place, load.slot))
                if old:
                    sp.wait_ge(blocks_used, old.uses[-1].number + 1)
                    if old.uses[0] in DEGREE_BLOCKS:
                        sp.wait_ge(deg_added, DEGREE_BLOCKS.index(old.uses[0]) + 1)
                last_in[load.place, load.slot] = load
                sp.dma_start(places[load.place][:, load.slot, :], adj[b.row.i, b.j])\
                    .then_inc(loaded[load.place][load.slot], 16)

        @block.gpsimd
        def _(pool):
            pool.memset(partial[:, :, :], 0.0).then_inc(cleared, 1)
            pool.memset(operand[:, :, F:2 * F], 0.0).then_inc(cleared, 1)
            for row in ROWS:
                if row.sweep == 3:
                    pool.wait_ge(norm_ready, row.r - 1 - NB)
                    pool.dma_start(u_in[:, row.r % 2], u[:, tiles(row.i), :]).then_inc(u_loaded[row.r % 2], 16)
                if row.sweep < SWEEPS:
                    pool.wait_ge(first_taken, row.r + 1)
                    pool.wait_ge(cleared, row.r + 2)
                    rows = half_of(row.half) if row.double else slice(0, P)
                    pool.memset(partial[rows, row.i, :], 0.0).then_inc(cleared, 1)

        @block.tensor
        def _(pe):
            waited = {}

            def wait_new(semaphore, value):
                if waited.get(semaphore.name, 0) < value:
                    waited[semaphore.name] = value
                    pe.wait_ge(semaphore, value)

            def tiles_of(b):
                return data_of(b).rearrange("p (t i) -> p t i", t=TPB)

            def one_product(b, acc):
                stream = tiles_of(b)
                for t in range(TPB):
                    last = nc.tensor.matmul(
                        acc[half_of(t % 2), :], operand[:, b.j * TPB + t, half_of(b.row.half)], stream[:, t, :],
                        start=b.first and t < 2, stop=b.last and t >= 2)
                return last

            def single(b):
                if b.first and b.row.r >= 2:
                    wait_new(first_taken, b.row.r - 1)
                return one_product(b, single_acc[b.row.r % 2])

            uses = [0]

            def next_spare():
                n = uses[0]
                uses[0] += 1
                if n >= 2:
                    what, count = SPARE_USES[n - 2]
                    wait_new({"added": added_taken, "turn": own_ready, "degree": deg_taken}[what], count + 1)
                return spare[n % 2]

            def two_products(b, acc):
                stream = tiles_of(b)
                for t in range(TPB):
                    last = nc.tensor.matmul(
                        acc[:, :], operand[:, b.j * TPB + t, :], stream[:, t, :],
                        start=b.first and t == 0, stop=b.last and t == TPB - 1)
                return last

            def double(b):
                if b.first and rows_with_doubles(b.row.r - 2):
                    wait_new(sums_ready, rows_with_doubles(b.row.r - 2))
                    wait_saved(wait_new, b.row.r - 2)
                return two_products(b, double_acc[b.row.r % 2])

            group_bank = [None]

            def early_or_late(b):
                if b.first:
                    group_bank[0] = next_spare()
                return (two_products if b.kind == "early" else one_product)(b, group_bank[0])

            def turn(row):
                wait_operand(wait_new, row.sweep, row.i)
                acc = next_spare()
                wait_new(cleared, 2)
                for t in range(TPB):
                    last = nc.tensor.transpose(acc[:, t * P:(t + 1) * P], operand[:, row.i * TPB + t, :], ident[:, :])
                last.then_inc(turned, 1)

            def post(row):
                if row.double:
                    wait_new(sums_ready, rows_with_doubles(row.r))
                else:
                    wait_new(first_taken, row.r + 1)
                if row.own:
                    wait_new(own_ready, rows_with_own(row.r))
                if row.r >= 2:
                    before = ROWS[row.r - 2]
                    if before.sweep <= 2:
                        wait_new(tanh_ready, before.r + 1)
                    else:
                        wait_new(natural_taken, before.r + 1 - 2 * NB)
                acc = natural[row.r % 2]
                mixed = row.own and row.sweep != SWEEPS
                for t in range(TPB):
                    cut = slice(t * P, (t + 1) * P)
                    last = nc.tensor.matmul(
                        acc[:, t * F:(t + 1) * F], sums[:, row.r % 2, cut], w_both_sb[:, row.sweep - 1, :],
                        start=True, stop=not mixed)
                    if row.own:
                        to = (t + (0 if mixed else TPB)) * F
                        last = nc.tensor.matmul(
                            acc[:, to:to + F], own_t[half_of(row.half), row.r % 2, cut],
                            w_own_sb[half_of(row.half), row.sweep // SWEEPS, :], start=not mixed, stop=True)
                last.then_inc(posted, 1)

            def degree(row):
                wait_new(deg_folded, DEGREE_ROWS.index(row) + 1)
                acc = next_spare()
                for t in range(TPB):
                    part = deg_part[:, DEGREE_ROWS.index(row) % 2, t * P:(t + 1) * P]
                    last = nc.tensor.matmul(acc[:, t:t + 1], part, ones_sb[:, :], start=True, stop=True)
                last.then_inc(deg_summed, 1)

            wait_new(consts_loaded, 16 * 5)
            for what, of in PLAN:
                if what == "block":
                    wait_operand(wait_new, of.row.sweep, of.j)
                    if of.kind in ("double", "early"):
                        wait_operand(wait_new, of.row.sweep + 1, of.j)
                    wait_loaded(wait_new, of)
                    multiply = {"single": single, "double": double, "early": early_or_late, "late": early_or_late}
                    multiply[of.kind](of).then_inc(blocks_used, 1)
                elif what in ("turn", "post", "degree"):
                    {"turn": turn, "post": post, "degree": degree}[what](of)

        @block.scalar
        def _(act):
            for to, of in ((w_both_sb, w_both), (w_own_sb, w_own), (bias_sb, bias), (ident, identity), (ones_sb, ones)):
                act.dma_start(to[:], of[:]).then_inc(consts_loaded, 16)

            deviations = [0]

            def deviation(n, slot):
                deviations[0] += 1
                act.wait_ge(var_ready, deviations[0])
                nc.scalar.activation(sd[:, slot, 0:n], moments[:, slot, 0:n, 1], ACT.Sqrt, bias=eps[:, 0:1]).then_inc(sd_ready, 1)

            act.wait_ge(eps_set, 1)
            for g in range(NGROUPS):
                deviation(GROUP, g % 2)
            for what, row in PLAN:
                if what == "block":
                    continue
                slot = row.r % 2
                if what == "doubles" and row.sweep > 1:
                    act.wait_ge(blocks_used, used(row, "double"))
                    act.wait_ge(first_taken, row.r + 1)
                    other = half_of(1 - row.half)
                    nc.scalar.copy(partial[other, row.i, :], double_acc[slot][other, :]).then_inc(partial_saved, 1)
                elif what == "turn":
                    act.wait_ge(turned, rows_with_own(row.r))
                    own = half_of(row.half)
                    use = SPARE_USES.index(("turn", rows_with_own(row.r) - 1))
                    nc.scalar.copy(own_t[own, slot, :], spare[use % 2][own, :]).then_inc(own_ready, 1)
                elif what == "post":
                    if row.sweep <= 2:
                        act.wait_ge(posted, row.r + 1)
                        got = natural[slot][:, 0:TPB * F].rearrange("p (t f) -> p t f", t=TPB)
                        to = operand[:, tiles(row.i), F:2 * F] if row.sweep == 1 else tanh_out[:, slot]
                        nc.scalar.activation(to, got, ACT.Tanh).then_inc(tanh_ready, 1)
                    if row.sweep in (2, 3, 4):
                        deviation(TPB, 0)
                    if row.sweep == SWEEPS:
                        act.wait_ge(natural_taken, row.r + 1 - 2 * NB)
                        act.dma_start(out[:, tiles(row.i), :], result[:, slot]).then_inc(out_stored[slot], 16)
            for s in out_stored:
                act.wait_ge(s, 16 * NB // 2)

        @block.vector
        def _(dve):
            steps = [0]

            def link(instruction):
                steps[0] += 1
                instruction.then_inc(step, 1)
                dve.wait_ge(step, steps[0])

            norms = [0]

            def variances(values, n, slot):
                for t in range(n):
                    last = nc.vector.bn_stats(stats[:, slot, t, :], values[:, t, :])
                link(last)
                for t in range(n):
                    last = nc.vector.bn_aggr(moments[:, slot, t, :], stats[:, slot, t, :])
                last.then_inc(var_ready, 1)

            def normalize(values, n, slot):
                norms[0] += 1
                dve.wait_ge(sd_ready, norms[0])
                link(nc.vector.reciprocal(rsd[:, 0:n], sd[:, slot, 0:n]))
                for t in range(n):
                    last = nc.vector.tensor_scalar(centred[:, t, :], values[:, t, :], moments[:, slot, t, 0:1],
                                                   rsd[:, t:t + 1], ALU.subtract, ALU.mult)
                link(last)

            def first_variances(g):
                dve.wait_ge(x_loaded[g], 16)
                variances(resid[:, g * GROUP:(g + 1) * GROUP, :], GROUP, g % 2)

            def first_operand(g):
                if g + 1 < NGROUPS:
                    first_variances(g + 1)
                cut = slice(g * GROUP, (g + 1) * GROUP)
                normalize(resid[:, cut, :], GROUP, g % 2)
                nc.vector.tensor_scalar_max(operand[:, cut, 0:F], centred[:, :, :], 0.0).then_inc(first_ready, 1)

            folds = [0]

            def add_degrees(n, b):
                acc, data = deg_part[:, DEGREE_ROWS.index(b.row) % 2, :], data_of(b)
                fresh = n == 0 or DEGREE_BLOCKS[n - 1].row is not b.row
                if fresh and DEGREE_ROWS.index(b.row) >= 2:
                    dve.wait_ge(deg_summed, DEGREE_ROWS.index(b.row) - 1)
                wait_loaded(dve.wait_ge, b)
                if fresh:
                    nc.vector.tensor_tensor(acc, data[:, 0:2 * BLOCK], data[:, 2 * BLOCK:], ALU.add)\
                        .then_inc(deg_added, 1)
                else:
                    link(nc.vector.tensor_tensor(acc, acc, data[:, 0:2 * BLOCK], ALU.add))
                    nc.vector.tensor_tensor(acc, acc, data[:, 2 * BLOCK:], ALU.add).then_inc(deg_added, 1)
                dve.wait_ge(deg_added, n + 1)
                if n + 1 == len(DEGREE_BLOCKS) or DEGREE_BLOCKS[n + 1].row is not b.row:
                    folds[0] += 1
                    nc.vector.tensor_tensor(acc[:, 0:BLOCK], acc[:, 0:BLOCK], acc[:, BLOCK:], ALU.add)\
                        .then_inc(deg_folded, 1)
                    dve.wait_ge(deg_folded, folds[0])

            def take_first(row):
                if row.r >= 2:
                    dve.wait_ge(posted, row.r - 1)
                to, before = sums[:, row.r % 2, :], partial[:, row.i, :]
                if row.single:
                    dve.wait_ge(blocks_used, used(row, "single"))
                    got = single_acc[row.r % 2]
                wait_partial(dve.wait_ge, row)
                if added_to(row):
                    dve.wait_ge(added_taken, added_to(row))
                if row.sweep == 1:
                    own, other = half_of(row.half), half_of(1 - row.half)
                    nc.vector.tensor_copy(to[other, :], got[other, :])
                    nc.vector.tensor_tensor(to[own, :], got[own, :], before[own, :], ALU.add).then_inc(first_taken, 1)
                elif row.single:
                    nc.vector.tensor_tensor(to, got[:, :], before, ALU.add).then_inc(first_taken, 1)
                else:
                    nc.vector.tensor_copy(to, before).then_inc(first_taken, 1)

            def take_doubles(row):
                dve.wait_ge(blocks_used, used(row, "double"))
                dve.wait_ge(first_taken, row.r + 1)
                own, other = half_of(row.half), half_of(1 - row.half)
                got, to = double_acc[row.r % 2], sums[own, row.r % 2, :]
                nc.vector.tensor_tensor(to, got[own, :], to, ALU.add).then_inc(sums_ready, 1)
                if row.sweep == 1:
                    saved = partial[other, row.i, :]
                    nc.vector.tensor_tensor(saved, got[other, :], saved, ALU.add).then_inc(partial_added, 1)

            def take_added(row, number, count):
                dve.wait_ge(blocks_used, number + 1)
                wait_partial(dve.wait_ge, row)
                if count:
                    dve.wait_ge(added_taken, count)
                got, to = spare[SPARE_USES.index(("added", count)) % 2], partial[:, row.i, :]
                nc.vector.tensor_tensor(to, got[:, :], to, ALU.add).then_inc(added_taken, 1)

            def take_degrees(row):
                count = DEGREE_ROWS.index(row)
                dve.wait_ge(deg_summed, count + 1)
                got = spare[SPARE_USES.index(("degree", count)) % 2][:, 0:TPB]
                to = deg_plus[:, tiles(row.i)]
                if row.sweep == 1:
                    nc.vector.tensor_scalar_add(to, got, 1.0).then_inc(deg_taken, 1)
                else:
                    dve.wait_ge(deg_taken, count)
                    nc.vector.tensor_tensor(to, got, to, ALU.add).then_inc(deg_taken, 1)
                if row is DEGREE_ROWS[-1]:
                    dve.wait_ge(deg_taken, count + 1)
                    link(nc.vector.reciprocal(rdeg[:, :], deg_plus[:, :]))

            def finish(row):
                slot, k = row.r % 2, row.r % NB
                got = natural[slot][:, 0:TPB * F].rearrange("p (t f) -> p t f", t=TPB)
                value = resid[:, tiles(row.i), :]
                if row.sweep == 2:
                    dve.wait_ge(tanh_ready, row.r + 1)
                    link(nc.vector.tensor_tensor(value, value, tanh_out[:, slot], ALU.add))
                if row.sweep == 3:
                    dve.wait_ge(u_loaded[slot], 16 * (k // 2 + 1))
                    dve.wait_ge(consts_loaded, 16 * 5)
                    nc.vector.tensor_scalar(keep[:, :, :], u_in[:, slot], P_DROP, 1.0 / (1.0 - P_DROP),
                                            ALU.is_ge, ALU.mult)
                    with_bias = bias_sb[:, :].unsqueeze(1).to_broadcast([P, TPB, F])
                    link(nc.vector.tensor_tensor(value, value, with_bias, ALU.add))
                if row.sweep in (3, 4):
                    dve.wait_ge(posted, row.r + 1)
                    nc.vector.tensor_tensor(value, got, value, ALU.add).then_inc(natural_taken, 1)
                    dve.wait_ge(natural_taken, row.r + 1 - 2 * NB)
                if row.sweep in (2, 4):
                    variances(value, TPB, 0)
                    normalize(value, TPB, 0)
                    nc.vector.tensor_scalar_max(operand[:, tiles(row.i), 0:F], centred[:, 0:TPB, :], 0.0)\
                        .then_inc(norm_ready, 1)
                if row.sweep == 3:
                    variances(value, TPB, 0)
                    normalize(value, TPB, 0)
                    nc.vector.scalar_tensor_tensor(operand[:, tiles(row.i), F:2 * F], centred[:, 0:TPB, :], 0.0,
                                                   keep[:, :, :], ALU.max, ALU.mult).then_inc(norm_ready, 1)
                if row.sweep == SWEEPS:
                    dve.wait_ge(posted, row.r + 1)
                    own = natural[slot][:, TPB * F:2 * TPB * F].rearrange("p (t f) -> p t f", t=TPB)
                    link(nc.vector.tensor_tensor(value, own, value, ALU.add))
                    if k >= 2:
                        dve.wait_ge(out_stored[slot], 16 * (k // 2))
                    for t in range(TPB):
                        at = row.i * TPB + t
                        last = nc.vector.scalar_tensor_tensor(result[:, slot, t], got[:, t, :], rdeg[:, at:at + 1],
                                                              value[:, t, :], ALU.mult, ALU.add)
                    last.then_inc(natural_taken, 1)

            nc.vector.memset(eps[:, :], EPS).then_inc(eps_set, 1)
            first_variances(0)
            for g in range(NGROUPS):
                first_operand(g)

            count = 0
            for what, of in PLAN:
                if what == "block":
                    number = of.number
                    if of in DEGREE_BLOCKS:
                        add_degrees(DEGREE_BLOCKS.index(of), of)
                elif what == "first":
                    take_first(of)
                elif what == "doubles":
                    take_doubles(of)
                elif what == "added":
                    take_added(of, number, count)
                    count += 1
                elif what == "post" and of.sweep > 1:
                    finish(of)
                elif what == "degree":
                    take_degrees(of)


def kernel(x, adj, L0_gnn_W, L1_gnn_weight, L1_gnn_bias, L2_gnn_u, L3_gnn_W):
    import numpy as np
    from concourse import bacc
    from concourse.bass_utils import run_bass_kernel_spmd

    def by_partition(a):
        return np.ascontiguousarray(np.asarray(a).reshape(NT, P, F).transpose(1, 0, 2))

    w0, w1 = np.asarray(L0_gnn_W)
    w3 = np.asarray(L3_gnn_W).T
    eye = np.eye(F, dtype=np.float32)
    both = [w0[:F], w1[:F], np.asarray(L1_gnn_weight), eye, w3[F:]]
    arrays = {
        "adj": np.ascontiguousarray(
            np.asarray(adj).reshape(NB, BLOCK, NB, TPB, P).transpose(0, 2, 4, 3, 1)
        ).reshape(NB, NB, P, TPB * BLOCK),
        "x": by_partition(x),
        "w_both": np.ascontiguousarray(np.stack([np.concatenate([w, w]) for w in both], axis=1)),
        "w_own": np.ascontiguousarray(np.stack([np.concatenate([w0[F:], w1[F:]]), np.concatenate([w3[:F], w3[:F]])], axis=1)),
        "bias": np.ascontiguousarray(np.broadcast_to(np.asarray(L1_gnn_bias), (P, F))),
        "u": by_partition(L2_gnn_u),
        "identity": np.eye(P, dtype=np.float32),
        "ones": np.ones((P, 1), np.float32),
    }
    nc = bacc.Bacc("TRN2", target_bir_lowering=False, num_devices=1)
    aps = {name: nc.dram_tensor("in_" + name, a.shape, mybir.dt.float32, kind="ExternalInput").ap()
           for name, a in arrays.items()}
    aps["out"] = nc.dram_tensor("out_rows", (P, NT, F), mybir.dt.float32, kind="ExternalOutput").ap()
    gnn_kernel(nc, **aps)
    got = run_bass_kernel_spmd(nc, [{"in_" + name: a for name, a in arrays.items()}], core_ids=[0])
    rows = got.results[0]["out_rows"]
    return np.ascontiguousarray(np.asarray(rows).transpose(1, 0, 2)).reshape(N, F)
```
